# Optimizing a Trainium2 kernel written in Bass

```python
import numpy as np
import jax
import jax.numpy as jnp

def _softmax(x, axis=-1):
    return jax.nn.softmax(x, axis=axis)

def _gelu(x):
    return jax.nn.gelu(x, approximate=True)

def _silu(x):
    return jax.nn.silu(x)

def _sigmoid(x):
    return jax.nn.sigmoid(x)

def _layernorm(x, axis=-1, eps=1e-05):
    m = jnp.mean(x, axis=axis, keepdims=True)
    v = jnp.var(x, axis=axis, keepdims=True)
    return (x - m) / jnp.sqrt(v + eps)

def _scatter_add(tgt, idx, src, axis=0):
    return tgt.at[idx].add(src)

def _segment_sum(src, seg, n):
    return jax.ops.segment_sum(src, seg, n)
kernel_name = 'mk_lm_tower_d1_tok_ids1024_r4_0f86dd'

def setup_inputs(seed: int=0):
    np.random.seed(seed)
    _w = jnp.asarray

    def _rec_inputs():
        import jax
        import jax.numpy as jnp
        _rk = jax.random.key(seed)
        x = jax.random.randint(jax.random.fold_in(_rk, 1), (2, 2048), 0, 12564, jnp.int32)
        return x
    x = _rec_inputs()

    def _L0_tok_setup():
        import jax, jax.numpy as jnp
        import numpy as np
        VOCAB = 50257
        NUM_DIM = 256
        BATCH = 4
        SEQ = 1024
        key = jax.random.key(seed)
        k_tok, k_w, k_b = jax.random.split(key, 3)
        tokens = jax.random.randint(k_tok, (BATCH, SEQ), 0, VOCAB)
        weight = jax.random.normal(k_w, (NUM_DIM, VOCAB), dtype=jnp.float32) * 0.02
        bias = jax.random.normal(k_b, (NUM_DIM,), dtype=jnp.float32) * 0.02
        return {'tokens': tokens, 'weight': weight, 'bias': bias}
    _L0_tok_all = _L0_tok_setup()
    _L0_tok_in = {k: v for k, v in _L0_tok_all.items() if k in ('weight', 'bias')}
    del _L0_tok_all

    def _L0_attn_setup():
        import jax, jax.numpy as jnp
        import numpy as np
        import math
        B, N, DIM, H, DH, NNULL = (2, 512, 256, 16, 64, 2)
        SCALE = 8.0
        LN_EPS = 1e-05

        def _alibi_slopes(heads):
            start = 2.0 ** (-2.0 ** (-(math.log2(heads) - 3)))
            return np.array([start * start ** i for i in range(heads)], dtype=np.float32)

        def _l2norm(t):
            n = jnp.sqrt(jnp.sum(t * t, axis=-1, keepdims=True))
            return t / jnp.maximum(n, 1e-12)
        key = jax.random.key(seed)
        ks = jax.random.split(key, 6)
        inner = H * DH
        return {'x': jax.random.normal(ks[0], (B, N, DIM), dtype=jnp.float32), 'norm_g': jnp.ones((DIM,), jnp.float32), 'norm_b': jnp.zeros((DIM,), jnp.float32), 'Wq': jax.random.normal(ks[1], (DIM, inner), jnp.float32) * 0.02, 'Wkv': jax.random.normal(ks[2], (DIM, 2 * inner), jnp.float32) * 0.02, 'q_scale': jnp.ones((DH,), jnp.float32), 'k_scale': jnp.ones((DH,), jnp.float32), 'null_kv': jax.random.normal(ks[3], (H, 2 * NNULL, DH), jnp.float32), 'Wout': jax.random.normal(ks[4], (inner, DIM), jnp.float32) * 0.02}
    _L0_attn_all = _L0_attn_setup()
    _L0_attn_in = {k: v for k, v in _L0_attn_all.items() if k in ('norm_g', 'norm_b', 'Wq', 'Wkv', 'q_scale', 'k_scale', 'null_kv', 'Wout')}
    del _L0_attn_all

    def _L0_ffn_setup():
        import jax, jax.numpy as jnp
        import numpy as np
        E = 8
        K = 2
        D = 256
        H = 256
        B, T = (2, 256)
        key = jax.random.key(seed)
        ks = jax.random.split(key, 6)
        s = 0.02
        return {'x': jax.random.normal(ks[0], (B, T, D), dtype=jnp.float32), 'gate_w': jax.random.normal(ks[1], (E, D), dtype=jnp.float32) * s, 'lb_bias': jnp.zeros((E,), dtype=jnp.float32), 'w1': jax.random.normal(ks[2], (E, H, D), dtype=jnp.float32) * s, 'w2': jax.random.normal(ks[3], (E, D, H), dtype=jnp.float32) * s, 'cfc': jax.random.normal(ks[4], (H, D), dtype=jnp.float32) * s, 'cproj': jax.random.normal(ks[5], (D, H), dtype=jnp.float32) * s}
    _L0_ffn_all = _L0_ffn_setup()
    _L0_ffn_in = {k: v for k, v in _L0_ffn_all.items() if k in ('gate_w', 'lb_bias', 'w1', 'w2', 'cfc', 'cproj')}
    del _L0_ffn_all
    return {'x': x, 'L0_tok_weight': _L0_tok_in['weight'], 'L0_tok_bias': _L0_tok_in['bias'], 'L0_attn_norm_g': _L0_attn_in['norm_g'], 'L0_attn_norm_b': _L0_attn_in['norm_b'], 'L0_attn_Wq': _L0_attn_in['Wq'], 'L0_attn_Wkv': _L0_attn_in['Wkv'], 'L0_attn_q_scale': _L0_attn_in['q_scale'], 'L0_attn_k_scale': _L0_attn_in['k_scale'], 'L0_attn_null_kv': _L0_attn_in['null_kv'], 'L0_attn_Wout': _L0_attn_in['Wout'], 'L0_ffn_gate_w': _L0_ffn_in['gate_w'], 'L0_ffn_lb_bias': _L0_ffn_in['lb_bias'], 'L0_ffn_w1': _L0_ffn_in['w1'], 'L0_ffn_w2': _L0_ffn_in['w2'], 'L0_ffn_cfc': _L0_ffn_in['cfc'], 'L0_ffn_cproj': _L0_ffn_in['cproj']}

def reference(x, L0_tok_weight, L0_tok_bias, L0_attn_norm_g, L0_attn_norm_b, L0_attn_Wq, L0_attn_Wkv, L0_attn_q_scale, L0_attn_k_scale, L0_attn_null_kv, L0_attn_Wout, L0_ffn_gate_w, L0_ffn_lb_bias, L0_ffn_w1, L0_ffn_w2, L0_ffn_cfc, L0_ffn_cproj):
    import jax
    import jax.numpy as jnp

    def _L0_tok_ref(tokens, weight, bias):
        import jax, jax.numpy as jnp
        import numpy as np
        VOCAB = 50257
        NUM_DIM = 256
        BATCH = 4
        SEQ = 1024
        table = weight.T
        return jnp.take(table, tokens, axis=0) + bias

    def _L0_attn_ref(x, norm_g, norm_b, Wq, Wkv, q_scale, k_scale, null_kv, Wout):
        import jax, jax.numpy as jnp
        import numpy as np
        import math
        B, N, DIM, H, DH, NNULL = (2, 512, 256, 16, 64, 2)
        SCALE = 8.0
        LN_EPS = 1e-05

        def _alibi_slopes(heads):
            start = 2.0 ** (-2.0 ** (-(math.log2(heads) - 3)))
            return np.array([start * start ** i for i in range(heads)], dtype=np.float32)

        def _l2norm(t):
            n = jnp.sqrt(jnp.sum(t * t, axis=-1, keepdims=True))
            return t / jnp.maximum(n, 1e-12)
        b, n, dim = x.shape
        h, dh, nn = (H, DH, NNULL)
        j = n + nn
        mu = jnp.mean(x, axis=-1, keepdims=True)
        var = jnp.mean((x - mu) ** 2, axis=-1, keepdims=True)
        xn = (x - mu) * jax.lax.rsqrt(var + LN_EPS) * norm_g + norm_b
        q = (xn @ Wq).reshape(b, n, h, dh).transpose(0, 2, 1, 3)
        kv = x @ Wkv
        k, v = jnp.split(kv, 2, axis=-1)
        k = k.reshape(b, n, h, dh).transpose(0, 2, 1, 3)
        v = v.reshape(b, n, h, dh).transpose(0, 2, 1, 3)
        null = null_kv.reshape(h, nn, 2, dh)
        nk = jnp.broadcast_to(null[:, :, 0, :][None], (b, h, nn, dh))
        nv = jnp.broadcast_to(null[:, :, 1, :][None], (b, h, nn, dh))
        k = jnp.concatenate([nk, k], axis=2)
        v = jnp.concatenate([nv, v], axis=2)
        q = _l2norm(q) * q_scale
        k = _l2norm(k) * k_scale
        sim = jnp.einsum('bhid,bhjd->bhij', q, k) * SCALE
        irow = jnp.arange(j - n, j)
        jcol = jnp.arange(j)
        bias = -jnp.abs(jcol[None, :] - irow[:, None]).astype(sim.dtype)
        slopes = jnp.asarray(_alibi_slopes(h))[:, None, None]
        sim = sim + slopes * bias
        causal = jnp.triu(jnp.ones((n, j), dtype=bool), k=j - n + 1)
        neg = jnp.finfo(sim.dtype).max
        sim = jnp.where(causal[None, None], -neg, sim)
        attn = jax.nn.softmax(sim, axis=-1)
        out = jnp.einsum('bhij,bhjd->bhid', attn, v)
        out = out.transpose(0, 2, 1, 3).reshape(b, n, h * dh)
        return out @ Wout

    def _L0_ffn_ref(x, gate_w, lb_bias, w1, w2, cfc, cproj):
        import jax, jax.numpy as jnp
        import numpy as np
        E = 8
        K = 2
        D = 256
        H = 256
        B, T = (2, 256)
        Bx, Tx, Dx = x.shape
        logits = jnp.einsum('btd,ed->bte', x, gate_w)
        _, idx = jax.lax.top_k(logits + lb_bias, K)
        sel_logits = jnp.take_along_axis(logits, idx, axis=-1)
        w = jax.nn.sigmoid(sel_logits)
        w = w / (jnp.sum(w, axis=-1, keepdims=True) + 1e-06)
        xf = x.reshape(-1, Dx)
        idxf = idx.reshape(-1, K)
        wf = w.reshape(-1, K)
        onehot = jax.nn.one_hot(idxf, E, dtype=wf.dtype)
        we = jnp.einsum('nke,nk->ne', onehot, wf)
        hidden = jnp.square(jax.nn.relu(jnp.einsum('nd,ehd->neh', xf, w1)))
        expert_out = jnp.einsum('neh,edh->ned', hidden, w2)
        moe_out = jnp.einsum('ned,ne->nd', expert_out, we).reshape(Bx, Tx, Dx)
        sh = jnp.square(jax.nn.relu(jnp.einsum('btd,hd->bth', x, cfc)))
        shared = jnp.einsum('bth,dh->btd', sh, cproj)
        return moe_out + shared
    h = _L0_tok_ref(x, L0_tok_weight, L0_tok_bias)
    h = h + _L0_attn_ref(_layernorm(h, axis=-1), L0_attn_norm_g, L0_attn_norm_b, L0_attn_Wq, L0_attn_Wkv, L0_attn_q_scale, L0_attn_k_scale, L0_attn_null_kv, L0_attn_Wout)
    h = h + _L0_ffn_ref(_layernorm(h, axis=-1), L0_ffn_gate_w, L0_ffn_lb_bias, L0_ffn_w1, L0_ffn_w2, L0_ffn_cfc, L0_ffn_cproj)
    return h

_drawn_inputs = setup_inputs


def setup_inputs(seed=0):
    import zlib

    import numpy as np

    out = dict(_drawn_inputs(seed))
    spreads = {'L0_attn_norm_g': (1.0, 0.2),
     'L0_attn_norm_b': (0.0, 0.317),
     'L0_attn_q_scale': (1.0, 0.2),
     'L0_attn_k_scale': (1.0, 0.2),
     'L0_ffn_lb_bias': (0.0, 0.1)}
    factors = {}
    for name, (base, spread) in spreads.items():
        noise = np.random.default_rng([zlib.crc32(name.encode()), seed]).standard_normal(out[name].shape)
        drawn = base * np.exp(spread * noise) if base else spread * noise
        out[name] = jnp.asarray(drawn.astype(out[name].dtype))
    for name, factor in factors.items():
        out[name] = (out[name] * factor).astype(out[name].dtype)
    return out
```

```python
import concourse.bass as bass
from concourse import mybir
from contextlib import ExitStack


def lm_tower_kernel(nc, x, table, tok_bias, norm_g, norm_b, Wq, Wkv, q_scale, k_scale, null_kv, Wout,
                    gate_w, lb_bias, w1, w2, cfc, cproj, out):
    fp32, fp16, bf16 = mybir.dt.float32, mybir.dt.float16, mybir.dt.bfloat16
    i32, u32 = mybir.dt.int32, mybir.dt.uint32
    ALU = mybir.AluOpType
    ACT = mybir.ActivationFunctionType
    AX = mybir.AxisListType

    NB, N = x.shape
    V, D = table.shape
    DH = q_scale.shape[0]
    H = Wq.shape[1] // DH
    NN = null_kv.shape[1] // 2
    E, HF = w1.shape[0], w1.shape[2]
    C = D // 128
    FC = HF // 128
    T = N // 128
    G = 4
    GW = G * 128
    NG = T // G
    NP = H // 2
    PG = T // 2
    EA = E + 1
    UNITS = sum((it // G) + 1 for it in range(T))
    BLKS = sum(1 + G * (ig + 1) for ig in range(NG))
    start = 2.0 ** -0.5
    SLOPE = [start * start ** i for i in range(H)]
    QK_SCALE = 8.0
    LN_EPS = 1e-5
    NEG = -1e30
    ROW_A, ROW_B = 64, 96

    ctx = ExitStack()
    with ctx:
        def sb(name, shape, dt=fp32):
            return ctx.enter_context(nc.sbuf_tensor(name, shape, dt))

        def sem(name):
            return ctx.enter_context(nc.semaphore(name))

        ident = sb("ident", [128, 128])
        ident16 = sb("ident16", [128, 128], fp16)
        identb = sb("identb", [128, 128], bf16)
        mask_a = sb("mask_a", [128, 128], bf16)
        mask_b = sb("mask_b", [128, 128], bf16)
        slopes = sb("slopes", [128, H])
        key_pos = sb("key_pos", [128, T + G])
        btab = sb("btab", [128, H, T])
        null_pos = sb("null_pos", [NN, NG])
        btab_null = sb("btab_null", [NN, H, NG])
        group_pos = sb("group_pos", [128, T])
        shift0 = sb("shift0", [128, H, T])
        ones16 = sb("ones16", [128, N], fp16)
        iota8 = sb("iota8", [128, E])
        bias_bc = sb("bias_bc", [128, D])
        g_col = sb("g_col", [128, C])
        b_col = sb("b_col", [128, C])
        scl_bc = sb("scl_bc", [128, 4, DH])
        lb_bc = sb("lb_bc", [128, E])
        gw = sb("gw", [128, C, E])
        w1s = sb("w1s", [128, EA, C, HF])
        w2s = sb("w2s", [128, EA, FC, D])
        null_k = sb("null_k", [H * NN, DH])
        null_sq = sb("null_sq", [H * NN, DH])
        null_n = sb("null_n", [H * NN, 1])
        null_blk = sb("null_blk", [H * NN, 2, DH], fp16)
        null_ka = sb("null_ka", [128, H * NN], fp16)
        null_kb = sb("null_kb", [128, H * NN], fp16)
        null_v = sb("null_v", [NN, NP, 3, DH])
        idx = sb("idx", [128, T], i32)
        h = sb("h", [128, T, D])
        xT = sb("xT", [128, C, N])
        xnT = sb("xnT", [128, C, N])
        xn = sb("xn", [128, 2, D])
        stats = sb("stats", [128, T, 6])
        mv = sb("mv", [128, T, 2])
        var = sb("var", [128, T])
        rstd = sb("rstd", [128, T])
        minus_half = sb("minus_half", [128, T])
        eps = sb("eps", [128, T])
        wqkv = sb("wqkv", [128, C, 3, 128])
        wo = sb("wo", [128, D])
        sq = sb("sq", [128, 2, 512])
        ssq = sb("ssq", [128, 8])
        nsq = sb("nsq", [128, 8])
        rnorm = sb("rnorm", [128, 8])
        tqk = sb("tqk", [128, 2, 512])
        tqs = sb("tqs", [128, 2, 512])
        blk = sb("blk", [128, 2, 2, 2, 2, 2, DH], fp16)
        halves = sb("halves", [128, 2 * N])
        xs = halves[:, :].rearrange("p (u d) -> p u d", d=D)
        qk_a = halves[:, :].bitcast(fp16).rearrange("p (z a n) -> p z a n", z=2, a=2)
        qb = sb("qb", [128, 2, N], fp16)
        kb = sb("kb", [128, 2, N], fp16)
        kan = sb("kan", [128, 2, NN], fp16)
        kbn = sb("kbn", [128, 2, NN], fp16)
        bt = sb("bt", [128, 2, T])
        btn = sb("btn", [NN, 2, NG])
        vn = sb("vn", [NN, 3, DH])
        vt = sb("vt", [128, T, 3, DH])
        mx = sb("mx", [128, T, NG + 1])
        rowmax = sb("rowmax", [128, T])
        aug = sb("aug", [128, 2, T, 33], fp16)
        probs = sb("probs", [128, 4, GW])
        rec = sb("rec", [128, GW])
        ot = sb("ot", [128, N])
        lg = sb("lg", [128, T, E])
        lgb = sb("lgb", [128, T, E])
        top = sb("top", [128, T, 8])
        topi = sb("topi", [128, T, 8], u32)
        topf = sb("topf", [128, T, 8])
        oh0 = sb("oh0", [128, T, E])
        oh1 = sb("oh1", [128, T, E])
        sig = sb("sig", [128, T, E])
        wsum = sb("wsum", [128, T])
        wmoe = sb("wmoe", [128, T, EA])
        relu = halves[:, 0:N].rearrange("p (z f n) -> p z f n", z=2, f=FC)
        hid = halves[:, N:2 * N].rearrange("p (z f n) -> p z f n", z=2, f=FC)

        ps = ctx.enter_context(nc.psum_tensor("ps", [128, 8, 512], fp32))

        def bank(b):
            return ps[:, b, :]

        def bank16(b):
            return ps[:, b, :].bitcast(fp16)

        c_par = sem("c_par")
        e_par = sem("e_par")
        c_pool = sem("c_pool")
        c_act = sem("c_act")
        c_dve = sem("c_dve")
        c_pe = sem("c_pe")
        chain = sem("chain")
        chain_a = sem("chain_a")
        idx_in = sem("idx_in")
        var_ready = sem("var_ready")
        var_eps = sem("var_eps")
        rstd_ready = sem("rstd_ready")
        ssq_ready = sem("ssq_ready")
        nsq_ready = sem("nsq_ready")
        rnorm_ready = sem("rnorm_ready")
        gathered = [sem(f"gathered{i}") for i in range(NG)]
        x_ready = sem("x_ready")
        xt_ready = sem("xt_ready")
        xt_out = sem("xt_out")
        wqkv_in = sem("wqkv_in")
        wo_in = sem("wo_in")
        proj_done = sem("proj_done")
        sq_ready = sem("sq_ready")
        v_read = sem("v_read")
        qk_read = sem("qk_read")
        scaled = sem("scaled")
        hi_ready = sem("hi_ready")
        blk_ready = sem("blk_ready")
        tr_done = sem("tr_done")
        ta_done = sem("ta_done")
        tb_done = sem("tb_done")
        null_ready = sem("null_ready")
        slope_row = sem("slope_row")
        a_ready = sem("a_ready")
        a_read = sem("a_read")
        aug_ready = sem("aug_ready")
        aug_tr = sem("aug_tr")
        aug_in = sem("aug_in")
        s_ready = sem("s_ready")
        exp_done = sem("exp_done")
        pv_done = sem("pv_done")
        o_read = sem("o_read")
        w_ready = sem("w_ready")
        w_added = sem("w_added")
        y_ready = sem("y_ready")
        yt_ready = sem("yt_ready")
        yt_out = sem("yt_out")
        gate_ready = sem("gate_ready")
        lg_ready = sem("lg_ready")
        ex_ready = sem("ex_ready")
        h1_ready = sem("h1_ready")
        relu_ready = sem("relu_ready")
        hid_ready = sem("hid_ready")
        h2_ready = sem("h2_ready")
        h2_added = sem("h2_added")
        stored = sem("stored")
        h_free = sem("h_free")
        waited = sem("waited")

        NPAR = 12

        def blocks():
            for ig in range(NG):
                yield ig, None
                for jt in range(G * (ig + 1)):
                    yield ig, jt

        def units():
            yield None, 0
            for it in range(T):
                for c in range(it // G + 1):
                    yield it, c

        def mixed():
            ends, m = {}, 0
            for ig in range(NG):
                m += 1 + G * (ig + 1)
                ends[m - 1] = ig
            for m in range(BLKS + 2):
                yield "main", m
                if m - 2 in ends:
                    yield "norm", ends[m - 2]
                if m < UNITS + 1:
                    yield "max", m

        def first_col(ig, jt):
            return 0 if jt is None else 128 * max(jt - G * ig, 0)

        LIFTED = dict(
            sp=(h_free,),
            pool=(scaled,),
            act=(xt_out, v_read, ta_done, aug_in, exp_done, yt_out),
            dve=(qk_read, blk_ready, tb_done, a_read, o_read, w_added, hid_ready, h2_added, x_ready),
            pe=(proj_done, tr_done, pv_done, w_ready, xt_ready, yt_ready, h2_ready))

        def up(count):
            return count + 1

        def apart(eng):
            eng.sem_inc(waited, 1)

        block = ctx.enter_context(nc.Block())

        @block.sync
        def _(sp):
            for s in LIFTED["sp"]:
                sp.sem_inc(s, 1)
            sp.dma_start(bias_bc[:, :], tok_bias.partition_broadcast(128)).then_inc(c_par, 16)
            with nc.allow_non_contiguous_dma(reason="small parameter columns"):
                sp.dma_start(g_col[:, :], norm_g.rearrange("(c p) -> p c", p=128)).then_inc(c_par, 16)
                sp.dma_start(b_col[:, :], norm_b.rearrange("(c p) -> p c", p=128)).then_inc(c_par, 16)
            for j in range(4):
                sp.dma_start(scl_bc[:, j, :], (q_scale if j < 2 else k_scale).partition_broadcast(128)).then_inc(c_par, 16)
            sp.dma_start(lb_bc[:, :], lb_bias.partition_broadcast(128)).then_inc(c_par, 16)
            sp.dma_start(gw[:, :, :], gate_w.rearrange("(c p) e -> p c e", p=128)).then_inc(c_par, 16)
            nkv = null_kv.rearrange("h (n t) d -> (h n) t d", t=2)
            sp.dma_start(null_k[:, :], nkv[:, 0, :]).then_inc(c_par, 16)
            nv = null_kv.rearrange("(q a) (n t) d -> n q a t d", t=2, a=2)
            for a in range(2):
                sp.dma_start(null_v[:, :, 2 * a, :], nv[:, :, a, 1, :]).then_inc(c_par, 16)
            wq_v = Wq.rearrange("(c p) (n m) -> p c n m", p=128, m=128)
            wkv_v = Wkv.rearrange("(c p) (z n m) -> p c z n m", p=128, m=128, z=2)
            wo_v = Wout.rearrange("(n p) d -> n p d", p=128)

            def load_experts():
                sp.dma_start(w1s[:, 0:E, :, :], w1.rearrange("e (c p) f -> p e c f", p=128)).then_inc(e_par, 16)
                sp.dma_start(w2s[:, 0:E, :, :], w2.rearrange("e (c p) d -> p e c d", p=128)).then_inc(e_par, 16)
                sp.dma_start(w1s[:, E, :, :], cfc.rearrange("(c p) f -> p c f", p=128)).then_inc(e_par, 16)
                sp.dma_start(w2s[:, E, :, :], cproj.rearrange("(c p) d -> p c d", p=128)).then_inc(e_par, 16)

            load_experts()
            with sp.Fori(0, NB) as b:
                sp.wait_ge(x_ready, up(b * T))
                with nc.allow_non_contiguous_dma(reason="token numbers"):
                    sp.dma_start(idx[:, :], x.rearrange("b (t p) -> b p t", p=128)[b, :, :]).then_inc(idx_in, 16)
                with sp.Fori(0, NP) as p:
                    t = b * NP + p
                    sp.wait_ge(proj_done, up(t * PG))
                    sp.dma_start(wqkv[:, :, 0, :], wq_v[:, :, p, :]).then_inc(wqkv_in, 16)
                    sp.dma_start(wqkv[:, :, 1, :], wkv_v[:, :, 0, p, :]).then_inc(wqkv_in, 16)
                    sp.dma_start(wqkv[:, :, 2, :], wkv_v[:, :, 1, p, :]).then_inc(wqkv_in, 16)
                    sp.wait_ge(w_ready, up(t * 2 * NG))
                    sp.dma_start(wo[:, :], wo_v[p, :, :]).then_inc(wo_in, 16)
                sp.wait_ge(h2_added, up((b + 1) * EA * T // 2))
                sp.dma_start(out.rearrange("b (t p) d -> b p t d", p=128)[b, :, :, :], h[:, :, :]).then_inc(stored, 16)
                sp.wait_ge(stored, 16 * (b + 1))
                sp.sem_inc(h_free, 1)

        @block.gpsimd
        def _(pool):
            for s in LIFTED["pool"]:
                pool.sem_inc(s, 1)
            n = [0]

            def made(ins):
                n[0] += 1
                ins.then_inc(c_pool, 1)
                pool.wait_ge(c_pool, n[0])

            def done():
                pool.wait_ge(c_pool, n[0])

            for m, v in ((ident, 0.0), (mask_a, 0.0), (mask_b, 0.0), (ones16, 1.0), (kb, 0.0), (qb, 0.0),
                         (aug, 0.0), (mx, NEG), (null_kb, 0.0), (minus_half, -0.5),
                         (eps, LN_EPS)):
                made(pool.memset(m[:], v))
            for i in range(H):
                made(pool.memset(slopes[:, i:i + 1], SLOPE[i]))
            made(pool.memset(vt[:, :, 1, :], 1.0))
            made(pool.memset(null_v[:, :, 1, :], 1.0))
            made(pool.memset(wmoe[:, :, E:E + 1], 1.0))
            done()
            made(pool.affine_select(out=ident[:, :], in_=ident[:, :], compare_op=ALU.not_equal, fill=1.0, base=0,
                                    pattern=[[-1, 128]], channel_multiplier=1))
            made(pool.affine_select(out=mask_a[:, :], in_=mask_a[:, :], compare_op=ALU.is_ge, fill=NEG, base=0,
                                    pattern=[[-1, 128]], channel_multiplier=1))
            made(pool.affine_select(out=mask_b[:, :], in_=mask_b[:, :], compare_op=ALU.is_ge, fill=NEG, base=0,
                                    pattern=[[1, 128]], channel_multiplier=-1))
            ok = dict(allow_small_or_imprecise_dtypes=True)
            made(pool.iota(key_pos[:, 0:T], pattern=[[128, T]], base=-128 * (T - G), channel_multiplier=1, **ok))
            made(pool.iota(null_pos[:, :], pattern=[[-GW, NG]], base=-NN, channel_multiplier=1, **ok))
            made(pool.iota(group_pos[:, :], pattern=[[GW, NG], [0, G]], base=0, channel_multiplier=0, **ok))
            made(pool.iota(iota8[:, :], pattern=[[1, E]], base=0, channel_multiplier=0, **ok))
            for hd in range(2):
                made(pool.iota(kb[ROW_A:ROW_A + 1, hd, :], pattern=[[1, N]], base=0, channel_multiplier=0, **ok))
                made(pool.memset(kb[ROW_B:ROW_B + 1, hd, :], 1.0))
            made(pool.iota(null_kb[ROW_A:ROW_A + 1, :], pattern=[[0, H], [1, NN]], base=-NN, channel_multiplier=0, **ok))
            made(pool.memset(null_kb[ROW_B:ROW_B + 1, :], 1.0))
            done()
            made(pool.tensor_tensor(btab[:, :, :], key_pos[:, 0:T].unsqueeze(1).to_broadcast([128, H, T]),
                                    slopes[:, :].unsqueeze(2).to_broadcast([128, H, T]), ALU.mult))
            made(pool.tensor_tensor(btab_null[:, :, :], null_pos[:, :].unsqueeze(1).to_broadcast([NN, H, NG]),
                                    slopes[0:NN, :].unsqueeze(2).to_broadcast([NN, H, NG]), ALU.mult))
            made(pool.tensor_tensor(shift0[:, :, :], group_pos[:, :].unsqueeze(1).to_broadcast([128, H, T]),
                                    slopes[:, :].unsqueeze(2).to_broadcast([128, H, T]), ALU.mult))
            made(pool.tensor_copy(ident16[:, :], ident[:, :]))
            made(pool.tensor_copy(identb[:, :], ident[:, :]))
            pool.wait_ge(c_par, 16 * NPAR)
            made(pool.tensor_scalar(scl_bc[:, 2:4, :], scl_bc[:, 2:4, :], QK_SCALE, None, ALU.mult))
            made(pool.tensor_tensor(null_sq[:, :], null_k[:, :], null_k[:, :], ALU.mult))
            done()
            POOL_CONSTS[0] = n[0]
            pool.wait_ge(c_dve, 1)
            pool.tensor_scalar(null_n[:, :], null_n[:, :], 1e-24, None, ALU.max).then_inc(c_pool, 1)
            pool.wait_ge(c_pool, n[0] + 1)
            pool.tensor_tensor(null_n[:, :], null_n[:, :], minus_half[0:H * NN, 0:1], ALU.pow).then_inc(c_pool, 1)

            def inverse_root(k):
                pool.wait_ge(var_ready, k + 1)
                pool.tensor_tensor(var[:, :], mv[:, :, 1], eps[:, :], ALU.add).then_inc(var_eps, 1)
                pool.wait_ge(var_eps, k + 1)
                pool.tensor_tensor(rstd[:, :], var[:, :], minus_half[:, :], ALU.pow).then_inc(rstd_ready, 1)

            with pool.Fori(0, NB) as b:
                pool.wait_ge(idx_in, 16 * (b + 1))
                pool.wait_ge(h_free, up(b))
                apart(pool)
                for u in range(T):
                    pool.indirect_dma_start(h[:, u, :], None, table[:, :],
                                            bass.IndirectOffsetOnAxis(ap=idx[:, u:u + 1], axis=0),
                                            bounds_check=V - 1, oob_is_err=False).then_inc(gathered[u // G], 16)
                inverse_root(b * 3)
                inverse_root(b * 3 + 1)
                with pool.Fori(0, NP) as p:
                    t = b * NP + p

                    def inverse_norm(g):
                        pool.wait_ge(ssq_ready, t * PG + g + 1)
                        apart(pool)
                        pool.tensor_scalar(nsq[:, :], ssq[:, :], 1e-24, None, ALU.max).then_inc(nsq_ready, 1)
                        pool.wait_ge(nsq_ready, t * PG + g + 1)
                        pool.tensor_tensor(rnorm[:, :], nsq[:, :], minus_half[:, 0:8], ALU.pow).then_inc(rnorm_ready, 1)

                    for g in range(PG):
                        inverse_norm(g)
                        pool.wait_ge(qk_read, up(t * PG + g + 1))
                        if g >= 2:
                            pool.wait_ge(blk_ready, up(t * PG + g - 1))
                        else:
                            pool.wait_ge(blk_ready, up(t * PG))
                        nc.gpsimd.tensor_tensor(tqs[:, g % 2, :].rearrange("p (u n) -> p u n", u=2),
                                                tqk[:, g % 2, :].rearrange("p (u n) -> p u n", u=2),
                                                scl_bc[:, :, :].rearrange("p a d -> p (a d)").unsqueeze(1).to_broadcast([128, 2, 4 * DH]),
                                                ALU.mult).then_inc(scaled, 1)
                inverse_root(b * 3 + 2)

        @block.scalar
        def _(act):
            for s in LIFTED["act"]:
                act.sem_inc(s, 1)
            na = [0]

            def link(ins):
                na[0] += 1
                ins.then_inc(chain_a, 1)
                act.wait_ge(chain_a, na[0])

            act.wait_ge(c_pe, 1)
            nc.scalar.activation(null_ka[:, :], bank16(0)[:, 0:H * NN], ACT.Copy).then_inc(c_act, 1)
            nc.scalar.activation(null_kb[0:64, :], bank16(0)[64:128, 0:H * NN], ACT.Copy).then_inc(c_act, 1)
            act.wait_ge(c_act, 2)

            with act.Fori(0, NB) as b:
                for u in range(T):
                    tok = slice(u * 128, u * 128 + 128)
                    act.wait_ge(xt_ready, up(b * T + u + 1))
                    nc.scalar.activation(xT[:, :, tok], bank(u % 2)[:, 0:C * 128].rearrange("p (c n) -> p c n", c=C), ACT.Copy)
                    for c in range(C):
                        last = nc.scalar.activation(xnT[:, c, tok], bank(u % 2)[:, (C + c) * 128:(C + c + 1) * 128], ACT.Identity,
                                                    bias=b_col[:, c:c + 1], scale=g_col[:, c:c + 1])
                    last.then_inc(xt_out, 1)

                with act.Fori(0, NP) as p:
                    t = b * NP + p

                    def square(g):
                        act.wait_ge(proj_done, up(t * PG + g + 1))
                        act.wait_ge(qk_read, up(t * PG + (g - 1 if g >= 2 else 0)))
                        nc.scalar.activation(sq[:, g % 2, :], bank((5, 0)[g % 2]), ACT.Square).then_inc(sq_ready, 1)
                        nc.scalar.activation(vt[:, 2 * g:2 * g + 2, 0:3:2, :],
                                             bank((7, 1)[g % 2])[:, 0:256].rearrange("p (u a d) -> p u a d", u=2, a=2),
                                             ACT.Copy).then_inc(v_read, 1)

                    def high(g):
                        act.wait_ge(scaled, up(t * PG + g + 1))
                        act.wait_ge(tr_done, up(t * PG + (g - 1 if g >= 2 else 0)))
                        for z in range(2):
                            last = nc.scalar.activation(
                                blk[:, g % 2, :, z, :, z, :],
                                tqs[:, g % 2, :].rearrange("p (u z a d) -> p u z a d", u=2, z=2, a=2)[:, :, z, :, :], ACT.Copy)
                        last.then_inc(hi_ready, 1)

                    def evac(g):
                        act.wait_ge(tr_done, up(t * PG + g + 1))
                        nc.scalar.activation(qk_a[:, :, :, g * 256:g * 256 + 256],
                                             bank16((6, 2)[g % 2]).rearrange("p (z a n) -> p z a n", z=2, a=2),
                                             ACT.Copy).then_inc(ta_done, 1)

                    for g in range(PG + 2):
                        if g < PG:
                            square(g)
                        if g == 0:
                            act.wait_ge(pv_done, up(t * 2 * BLKS))
                            nc.scalar.activation(kan[:, :, :].rearrange("p a n -> p (a n)"), null_ka[:, bass.ds(p * 2 * NN, 2 * NN)], ACT.Copy)
                            nc.scalar.activation(kbn[:, :, :].rearrange("p a n -> p (a n)"), null_kb[:, bass.ds(p * 2 * NN, 2 * NN)], ACT.Copy)
                            nc.scalar.activation(vn[:, :, :], null_v[:, p, :, :], ACT.Copy)
                            nc.scalar.activation(bt[:, :, :], btab[:, bass.ds(p * 2, 2), :], ACT.Copy)
                            nc.scalar.activation(btn[:, :, :], btab_null[:, bass.ds(p * 2, 2), :], ACT.Copy).then_inc(null_ready, 1)
                        if 1 <= g <= PG:
                            high(g - 1)
                        if g >= 2:
                            evac(g - 2)
                    act.wait_ge(null_ready, t + 1)
                    m = 0
                    for hd in range(2):
                        for z in range(2):
                            act.wait_ge(aug_tr, t * 4 + 2 * hd + z + 1)
                            nc.scalar.activation(qb[ROW_A:ROW_A + 33, hd, z * (N // 2):(z + 1) * (N // 2)],
                                                 bank16((6, 7)[z])[0:33, :], ACT.Copy).then_inc(aug_in, 1)
                        for ig, jt in blocks():
                            w = GW - first_col(ig, jt)
                            act.wait_ge(s_ready, t * 2 * BLKS + m + 1)
                            act.wait_ge(pv_done, up(t * 2 * BLKS + (m - 3 if m >= 4 else 0)))
                            if jt is None:
                                nc.scalar.activation(probs[0:NN, m % 4, 0:w], bank(2 + m % 2)[0:NN, 0:w], ACT.Exp,
                                                     bias=btn[:, hd, ig:ig + 1]).then_inc(exp_done, 1)
                            else:
                                z = jt - G * ig + T - G
                                nc.scalar.activation(probs[:, m % 4, 0:w], bank(2 + m % 2)[:, 0:w], ACT.Exp,
                                                     bias=bt[:, hd, z:z + 1]).then_inc(exp_done, 1)
                            m += 1

                for u in range(T):
                    act.wait_ge(yt_ready, up(b * T + u + 1))
                    nc.scalar.activation(xT[:, :, u * 128:u * 128 + 128],
                                         bank(u % 2)[:, 0:C * 128].rearrange("p (c n) -> p c n", c=C), ACT.Copy).then_inc(yt_out, 1)
                act.wait_ge(lg_ready, b + 1)
                nc.scalar.activation(sig[:, :, :], lg[:, :, :], ACT.Exp, scale=-1.0).then_inc(ex_ready, 1)
                m = 0
                for e in range(EA):
                    for ig in range(NG):
                        act.wait_ge(h1_ready, (b * EA * NG) + m + 1)
                        act.wait_ge(hid_ready, up((b * EA * NG) + (m - 1 if m >= 2 else 0)))
                        z = 2 * (m % 2)
                        nc.scalar.activation(relu[:, m % 2, :, :], ps[:, z:z + FC, :], ACT.Relu).then_inc(relu_ready, 1)
                        m += 1

        @block.vector
        def _(dve):
            for s in LIFTED["dve"]:
                dve.sem_inc(s, 1)
            nd = [0]

            def link(ins):
                nd[0] += 1
                ins.then_inc(chain, 1)
                dve.wait_ge(chain, nd[0])

            dve.wait_ge(c_pool, POOL_CONSTS[0])
            nc.vector.tensor_reduce(null_n[:, :], null_sq[:, :], AX.X, ALU.add).then_inc(c_dve, 1)
            dve.wait_ge(c_pool, POOL_CONSTS[0] + 2)
            link(nc.vector.tensor_scalar(null_k[:, :], null_k[:, :], null_n[:, 0:1], None, ALU.mult))
            link(nc.vector.tensor_tensor(null_k[:, :], null_k[:, :], scl_bc[0:H * NN, 2, :], ALU.mult))
            link(nc.vector.tensor_copy(null_blk[:, 1, :], null_k[:, :]))
            link(nc.vector.tensor_tensor(null_blk[:, 0, :], null_k[:, :], null_blk[:, 1, :], ALU.subtract))
            nc.vector.tensor_copy(topf[:, 0, :], iota8[:, :]).then_inc(c_dve, 1)
            dve.wait_ge(c_dve, 2)
            apart(dve)
            dve.sem_clear(chain)

            def step(ins):
                nd[0] += 1
                ins.then_inc(chain, 1)
                return nd[0]

            def norm_stats(k, rows):
                got = [step(nc.vector.bn_stats(stats[:, u, :], rows[:, u, :])) for u in range(T)]
                for u in range(T):
                    dve.wait_ge(chain, got[u])
                    last = nc.vector.bn_aggr(mv[:, u, :], stats[:, u, :])
                last.then_inc(var_ready, 1)
                dve.wait_ge(rstd_ready, k + 1)

            with dve.Fori(0, NB) as b:
                nd[0] = 0
                for u in range(T):
                    if u % G == 0:
                        dve.wait_ge(gathered[u // G], (b + 1) * 16 * G)
                    step(nc.vector.tensor_tensor(h[:, u, :], h[:, u, :], bias_bc[:, :], ALU.add))
                dve.wait_ge(chain, nd[0])
                norm_stats(b * 3, h)
                for u in range(T):
                    step(nc.vector.tensor_scalar(xs[:, u, :], h[:, u, :], mv[:, u, 0:1], rstd[:, u:u + 1], ALU.subtract, ALU.mult))
                dve.wait_ge(chain, nd[0])
                norm_stats(b * 3 + 1, xs)
                for u in range(T):
                    dve.wait_ge(xt_ready, up(b * T + (u - 1 if u >= 2 else 0)))
                    nc.vector.tensor_scalar(xn[:, u % 2, :], xs[:, u, :], mv[:, u, 0:1], rstd[:, u:u + 1],
                                            ALU.subtract, ALU.mult).then_inc(x_ready, 1)
                apart(dve)
                dve.sem_clear(chain)

                with dve.Fori(0, NP) as p:
                    t = b * NP + p
                    nd[0] = 0

                    def norms(g):
                        dve.wait_ge(sq_ready, t * PG + g + 1)
                        nc.vector.tensor_reduce(ssq[:, :], sq[:, g % 2, :].rearrange("p (a d) -> p a d", d=DH),
                                                AX.X, ALU.add).then_inc(ssq_ready, 1)
                        dve.wait_ge(rnorm_ready, t * PG + g + 1)
                        dve.wait_ge(scaled, up(t * PG + (g - 1 if g >= 2 else 0)))
                        nc.vector.tensor_tensor(tqk[:, g % 2, :].rearrange("p (a d) -> p a d", d=DH),
                                                bank((5, 0)[g % 2]).rearrange("p (a d) -> p a d", d=DH),
                                                rnorm[:, :].unsqueeze(2).to_broadcast([128, 8, DH]), ALU.mult).then_inc(qk_read, 1)

                    def low(g):
                        dve.wait_ge(hi_ready, t * PG + g + 1)
                        for z in range(2):
                            last = nc.vector.tensor_tensor(
                                blk[:, g % 2, :, z, :, 1 - z, :],
                                tqs[:, g % 2, :].rearrange("p (u z a d) -> p u z a d", u=2, z=2, a=2)[:, :, z, :, :],
                                blk[:, g % 2, :, z, :, z, :], ALU.subtract)
                        last.then_inc(blk_ready, 1)

                    def evac(g):
                        dve.wait_ge(ta_done, up(t * PG + g + 1))
                        src = bank16((6, 2)[g % 2]).rearrange("p (z a n) -> p z a n", z=2, a=2)
                        nc.vector.tensor_copy(qb[0:64, :, g * 256:g * 256 + 256], src[0:64, 0, :, :])
                        nc.vector.tensor_copy(kb[0:64, :, g * 256:g * 256 + 256], src[64:128, 1, :, :]).then_inc(tb_done, 1)

                    for g in range(PG + 2):
                        if g < PG:
                            norms(g)
                        if 1 <= g <= PG:
                            low(g - 1)
                        if g >= 2:
                            evac(g - 2)
                    for hd in range(2):
                        nc.vector.tensor_scalar(qb[ROW_A:ROW_A + 1, hd, :], ones16[ROW_A:ROW_A + 1, :],
                                                slopes[ROW_A:ROW_A + 1, bass.ds(2 * p + hd, 1)], None, ALU.mult).then_inc(slope_row, 1)
                    def unit_max(hd, n):
                        it, c = list(units())[n]
                        k = hd * (UNITS + 1) + n
                        dve.wait_ge(a_ready, t * 2 * (UNITS + 1) + k + 1)
                        if it is None:
                            nc.vector.tensor_reduce(mx[:, :, NG:NG + 1], bank(7)[:, 0:T * NN].rearrange("p (u n) -> p u n", n=NN),
                                                    AX.X, ALU.max).then_inc(a_read, 1)
                        else:
                            w = min(512, 128 * (it + 1) - 512 * c)
                            nc.vector.tensor_reduce(mx[:, it, c:c + 1], bank(k % 2)[:, 0:w], AX.X, ALU.max).then_inc(a_read, 1)

                    def shifts(hd):
                        dve.wait_ge(a_read, up(t * 2 * (UNITS + 1) + (hd + 1) * (UNITS + 1)))
                        link(nc.vector.tensor_reduce(rowmax[:, :], mx[:, :, :], AX.X, ALU.max))
                        nc.vector.tensor_tensor(aug[:, hd, :, 32:33].rearrange("p u n -> p (u n)"), shift0[:, 2 * p + hd, :],
                                                rowmax[:, :], ALU.subtract).then_inc(aug_ready, 1)
                        dve.wait_ge(aug_ready, 2 * t + hd + 1)

                    def normalise(hd, ig):
                        m = hd * BLKS + sum(1 + G * (i + 1) for i in range(ig + 1))
                        dve.wait_ge(pv_done, up(t * 2 * BLKS + m))
                        mine, sums = slice(hd * DH, hd * DH + DH), slice(DH - hd * DH, 2 * DH - hd * DH)
                        link(nc.vector.reciprocal(rec[mine, :], bank(4 + ig % 2)[sums, :]))
                        nc.vector.tensor_tensor(ot[mine, ig * GW:ig * GW + GW], bank(4 + ig % 2)[mine, :], rec[mine, :],
                                                ALU.mult).then_inc(o_read, 1)
                        dve.wait_ge(o_read, up(t * 2 * NG + hd * NG + ig + 1))

                    for n in range(UNITS + 1):
                        unit_max(0, n)
                    shifts(0)
                    for what, n in mixed():
                        if what == "max":
                            unit_max(1, n)
                        elif what == "norm":
                            normalise(0, n)
                        if what == "max" and n == UNITS:
                            shifts(1)
                    for ig in range(NG):
                        normalise(1, ig)
                    for k in range(2 * NG):
                        dve.wait_ge(w_ready, up(t * 2 * NG + k + 1))
                        hh = h[:, 2 * k:2 * k + 2, :].rearrange("p u d -> p (u d)")
                        nc.vector.tensor_tensor(hh, bank(6 + k % 2), hh, ALU.add).then_inc(w_added, 1)
                    dve.wait_ge(w_added, up(t * 2 * NG + 2 * NG))
                    apart(dve)
                    dve.sem_clear(chain)

                nd[0] = 0
                norm_stats(b * 3 + 2, h)
                for u in range(T):
                    nc.vector.tensor_scalar(xs[:, u, :], h[:, u, :], mv[:, u, 0:1], rstd[:, u:u + 1],
                                            ALU.subtract, ALU.mult).then_inc(y_ready, 1)
                dve.wait_ge(gate_ready, b + 1)
                logit = bank(2)[:, 0:T * E].rearrange("p (u e) -> p u e", e=E)
                nc.vector.tensor_copy(lg[:, :, :], logit).then_inc(lg_ready, 1)
                dve.wait_ge(lg_ready, b + 1)
                link(nc.vector.tensor_tensor(lgb[:, :, :], lg[:, :, :], lb_bc[:, :].unsqueeze(1).to_broadcast([128, T, E]), ALU.add))
                for u in range(T):
                    link(nc.vector.max(top[:, u, :], lgb[:, u, :]))
                    link(nc.vector.max_index(topi[:, u, :], top[:, u, :], lgb[:, u, :]))
                link(nc.vector.tensor_copy(topf[:, :, :], topi[:, :, :]))
                for z, m in ((0, oh0), (1, oh1)):
                    link(nc.vector.tensor_tensor(m[:, :, :], iota8[:, :].unsqueeze(1).to_broadcast([128, T, E]),
                                                 topf[:, :, z:z + 1].to_broadcast([128, T, E]), ALU.is_equal))
                link(nc.vector.tensor_tensor(oh0[:, :, :], oh0[:, :, :], oh1[:, :, :], ALU.add))
                dve.wait_ge(ex_ready, b + 1)
                link(nc.vector.tensor_scalar(sig[:, :, :], sig[:, :, :], 1.0, None, ALU.add))
                link(nc.vector.reciprocal(sig[:, :, :], sig[:, :, :]))
                link(nc.vector.tensor_tensor(sig[:, :, :], sig[:, :, :], oh0[:, :, :], ALU.mult))
                link(nc.vector.tensor_reduce(wsum[:, :], sig[:, :, :], AX.X, ALU.add))
                link(nc.vector.tensor_scalar(wsum[:, :], wsum[:, :], 1e-6, None, ALU.add))
                link(nc.vector.reciprocal(wsum[:, :], wsum[:, :]))
                link(nc.vector.tensor_tensor(wmoe[:, :, 0:E], sig[:, :, :], wsum[:, :].unsqueeze(2).to_broadcast([128, T, E]), ALU.mult))

                def square(m):
                    dve.wait_ge(relu_ready, b * EA * NG + m + 1)
                    dve.wait_ge(h2_ready, up(b * EA * T // 2 + (2 * (m - 1) if m >= 2 else 0)))
                    z = 2 * (m % 2)
                    nc.vector.scalar_tensor_tensor(out=hid[:, m % 2, :, :], in0=ps[:, z:z + FC, :], scalar=0.0,
                                                   in1=relu[:, m % 2, :, :], op0=ALU.max, op1=ALU.mult).then_inc(hid_ready, 1)

                def add(m):
                    e, ig = divmod(m, NG)
                    for k in range(2):
                        dve.wait_ge(h2_ready, up(b * EA * T // 2 + 2 * m + k + 1))
                        for s in range(2):
                            u = G * ig + 2 * k + s
                            last = nc.vector.scalar_tensor_tensor(out=h[:, u, :], in0=bank(4 + (2 * m + k) % 4)[:, s * D:s * D + D],
                                                                  scalar=wmoe[:, u, e:e + 1], in1=h[:, u, :], op0=ALU.mult, op1=ALU.add)
                        last.then_inc(h2_added, 1)

                for m in range(EA * NG + 1):
                    if m < EA * NG:
                        square(m)
                    if m % NG == 0:
                        dve.wait_ge(h2_added, up(b * EA * T // 2 + (2 * (m - 1) if m else 0)))
                    if m >= 1:
                        add(m - 1)
                dve.wait_ge(h2_added, up((b + 1) * EA * T // 2))
                apart(dve)
                dve.sem_clear(chain)

        @block.tensor
        def _(pe):
            for s in LIFTED["pe"]:
                pe.sem_inc(s, 1)
            mm = nc.tensor.matmul
            pe.wait_ge(c_pool, POOL_CONSTS[0])
            pe.wait_ge(c_dve, 2)
            nc.tensor.transpose(bank16(0)[:, 0:H * NN], null_blk[:, :, :].rearrange("p a d -> p (a d)"),
                                ident16[0:H * NN, 0:H * NN]).then_inc(c_pe, 1)
            pe.wait_ge(c_act, 2)

            with pe.Fori(0, NB) as b:
                for u in range(T):
                    pe.wait_ge(x_ready, up(b * T + u + 1))
                    pe.wait_ge(xt_out, up(b * T + (u - 1 if u >= 2 else 0)))
                    for z in range(2 * C):
                        src = xs[:, u, :] if z < C else xn[:, u % 2, :]
                        last = nc.tensor.transpose(bank(u % 2)[:, z * 128:z * 128 + 128],
                                                   src[:, (z % C) * 128:(z % C) * 128 + 128], ident[:, :])
                    last.then_inc(xt_ready, 1)
                pe.wait_ge(xt_out, up((b + 1) * T))
                apart(pe)

                with pe.Fori(0, NP) as p:
                    t = b * NP + p

                    def project(g):
                        if g == 0:
                            pe.wait_ge(wqkv_in, 48 * (t + 1))
                            pe.wait_ge(w_added, up(t * 2 * NG))
                        pe.wait_ge(qk_read, up(t * PG + (g - 1 if g >= 2 else 0)))
                        pe.wait_ge(v_read, up(t * PG + (g - 1 if g >= 2 else 0)))
                        for s in range(2):
                            tok = slice((2 * g + s) * 128, (2 * g + s + 1) * 128)
                            for z, src in enumerate((xnT, xT, xT)):
                                dst = bank((5, 0)[g % 2])[:, s * 256 + z * 128:s * 256 + z * 128 + 128] if z < 2 else \
                                    bank((7, 1)[g % 2])[:, s * 128:s * 128 + 128]
                                for c in range(C):
                                    last = mm(dst, src[:, c, tok], wqkv[:, c, z, :], start=(c == 0), stop=(c == C - 1))
                        last.then_inc(proj_done, 1)

                    def turn(g):
                        pe.wait_ge(blk_ready, up(t * PG + g + 1))
                        pe.wait_ge(tb_done, up(t * PG + (g - 1 if g >= 2 else 0)))
                        dst = bank16((6, 2)[g % 2]).rearrange("p (z a s n) -> p z a s n", z=2, a=2, s=2)
                        for z in range(2):
                            for hd in range(2):
                                for s in range(2):
                                    last = nc.tensor.transpose(dst[:, z, hd, s, :],
                                                               blk[:, g % 2, s, z, hd, :, :].rearrange("p a d -> p (a d)"), ident16[:, :])
                        last.then_inc(tr_done, 1)

                    for g in range(PG + 1):
                        if g < PG:
                            project(g)
                        if g >= 1:
                            turn(g - 1)

                    pe.wait_ge(ta_done, up((t + 1) * PG))
                    pe.wait_ge(tb_done, up((t + 1) * PG))
                    pe.wait_ge(v_read, up((t + 1) * PG))
                    pe.wait_ge(null_ready, t + 1)
                    def unit_scores(hd, n):
                        it, c = list(units())[n]
                        k = hd * (UNITS + 1) + n
                        base = t * 2 * (UNITS + 1)
                        if it is None:
                            pe.wait_ge(slope_row, 2 * t + hd + 1)
                            pe.wait_ge(a_read, up(base + k))
                            for u in range(T):
                                last = mm(bank(7)[:, u * NN:u * NN + NN], qb[0:ROW_A + 1, hd, u * 128:u * 128 + 128],
                                          kbn[0:ROW_A + 1, hd, :], start=True, stop=True)
                        else:
                            w = min(512, 128 * (it + 1) - 512 * c)
                            diag = c == it // G
                            pe.wait_ge(a_read, up(base + (k - 1)))
                            last = mm(bank(k % 2)[:, 0:w], qb[0:ROW_A + 1, hd, it * 128:it * 128 + 128],
                                      kb[0:ROW_A + 1, hd, c * 512:c * 512 + w], start=True, stop=not diag)
                            if diag:
                                last = mm(bank(k % 2)[:, w - 128:w], identb[:, :], mask_a[:, :], start=False, stop=True)
                        last.then_inc(a_ready, 1)

                    def turn_shifts(hd):
                        pe.wait_ge(aug_ready, 2 * t + hd + 1)
                        apart(pe)
                        for z in range(2):
                            for u in range(T // 2):
                                last = nc.tensor.transpose(bank16((6, 7)[z])[0:33, u * 128:u * 128 + 128], aug[:, hd, z * T // 2 + u, :],
                                                           ident16[:, :])
                            last.then_inc(aug_tr, 1)
                        pe.wait_ge(aug_in, up(4 * t + 2 * hd + 2))

                    todo = [(hd, ig, jt) for hd in range(2) for ig, jt in blocks()]

                    def scores(m):
                        hd, ig, jt = todo[m]
                        c0 = first_col(ig, jt)
                        w = GW - c0
                        q = slice(ig * GW + c0, ig * GW + GW)
                        pe.wait_ge(exp_done, up(t * 2 * BLKS + (m - 1 if m >= 2 else 0)))
                        if jt is None:
                            mm(bank(2 + m % 2)[0:NN, 0:w], kan[:, hd, :], qk_a[:, 0, hd, q], start=True, stop=False)
                            last = mm(bank(2 + m % 2)[0:NN, 0:w], kbn[0:ROW_B + 1, hd, :], qb[0:ROW_B + 1, hd, q], start=False, stop=True)
                        else:
                            j = slice(jt * 128, jt * 128 + 128)
                            dst = bank(2 + m % 2)
                            diag = jt >= G * ig
                            mm(dst[:, 0:w], qk_a[:, 1, hd, j], qk_a[:, 0, hd, q], start=True, stop=False)
                            last = mm(dst[:, 0:w], kb[0:ROW_B + 1, hd, j], qb[0:ROW_B + 1, hd, q], start=False, stop=not diag)
                            if diag:
                                last = mm(dst[:, 0:128], identb[:, :], mask_b[:, :], start=False, stop=True)
                        last.then_inc(s_ready, 1)

                    def products(m):
                        hd, ig, jt = todo[m]
                        c0 = first_col(ig, jt)
                        pe.wait_ge(exp_done, up(t * 2 * BLKS + m + 1))
                        o = bank(4 + ig % 2)
                        if jt is None:
                            n = hd * NG + ig
                            pe.wait_ge(o_read, up(t * 2 * NG + (n - 1 if n >= 2 else 0)))
                            last = mm(o, vn[:, hd:hd + 2, :].rearrange("p a d -> p (a d)"), probs[0:NN, m % 4, :], start=True, stop=False)
                        else:
                            last = mm(o[:, c0:GW], vt[:, jt, hd:hd + 2, :].rearrange("p a d -> p (a d)"), probs[:, m % 4, 0:GW - c0],
                                      start=False, stop=(jt == G * ig + G - 1))
                        last.then_inc(pv_done, 1)

                    for n in range(UNITS + 1):
                        unit_scores(0, n)
                    turn_shifts(0)
                    for what, n in mixed():
                        if what == "main":
                            if n < BLKS:
                                scores(n)
                            if n >= 2:
                                products(n - 2)
                        elif what == "max":
                            unit_scores(1, n)
                    turn_shifts(1)
                    for m in range(BLKS, 2 * BLKS + 2):
                        if m < 2 * BLKS:
                            scores(m)
                        if m >= BLKS + 2:
                            products(m - 2)

                    pe.wait_ge(wo_in, 16 * (t + 1))
                    pe.wait_ge(o_read, up((t + 1) * 2 * NG))

                    for k in range(2 * NG):
                        pe.wait_ge(w_added, up(t * 2 * NG + (k - 1 if k >= 2 else 0)))
                        for s in range(2):
                            last = mm(bank(6 + k % 2)[:, s * D:s * D + D], ot[:, (2 * k + s) * 128:(2 * k + s + 1) * 128],
                                      wo[:, :], start=True, stop=True)
                        last.then_inc(w_ready, 1)
                pe.wait_ge(w_added, up((b + 1) * NP * 2 * NG))

                pe.wait_ge(e_par, 64)
                for u in range(T + 1):
                    if u < T:
                        pe.wait_ge(y_ready, b * T + u + 1)
                        pe.wait_ge(yt_out, up(b * T + (u - 1 if u >= 2 else 0)))
                        for c in range(C):
                            last = nc.tensor.transpose(bank(u % 2)[:, c * 128:c * 128 + 128], xs[:, u, c * 128:c * 128 + 128], ident[:, :])
                        last.then_inc(yt_ready, 1)
                    if u >= 1:
                        pe.wait_ge(yt_out, up(b * T + u))
                        for c in range(C):
                            last = mm(bank(2)[:, (u - 1) * E:u * E], xT[:, c, (u - 1) * 128:u * 128], gw[:, c, :], start=(c == 0), stop=(c == C - 1))
                last.then_inc(gate_ready, 1)
                pe.wait_ge(lg_ready, b + 1)
                pe.wait_ge(ex_ready, b + 1)

                def first(m):
                    e, ig = divmod(m, NG)
                    pe.wait_ge(hid_ready, up(b * EA * NG + (m - 1 if m >= 2 else 0)))
                    for f in range(FC):
                        for c in range(C):
                            last = mm(bank(2 * (m % 2) + f), w1s[:, e, c, f * 128:f * 128 + 128], xT[:, c, ig * GW:ig * GW + GW],
                                      start=(c == 0), stop=(c == C - 1))
                    last.then_inc(h1_ready, 1)

                def second(m):
                    e, ig = divmod(m, NG)
                    pe.wait_ge(hid_ready, up(b * EA * NG + m + 1))
                    for z in range(2):
                        k = 2 * m + z
                        pe.wait_ge(h2_added, up(b * EA * T // 2 + (k - 3 if k >= 4 else 0)))
                        for s in range(2):
                            for f in range(FC):
                                last = mm(bank(4 + k % 4)[:, s * D:s * D + D], hid[:, m % 2, f, (2 * z + s) * 128:(2 * z + s + 1) * 128],
                                          w2s[:, e, f, :], start=(f == 0), stop=(f == FC - 1))
                        last.then_inc(h2_ready, 1)

                for m in range(EA * NG + 1):
                    if m < EA * NG:
                        first(m)
                    if m >= 1:
                        second(m - 1)
                pe.wait_ge(h2_added, up((b + 1) * EA * T // 2))


POOL_CONSTS = [0]

_NAMES = ["x", "table", "tok_bias", "norm_g", "norm_b", "Wq", "Wkv", "q_scale", "k_scale", "null_kv", "Wout",
          "gate_w", "lb_bias", "w1", "w2", "cfc", "cproj"]


def kernel(x, L0_tok_weight, L0_tok_bias, L0_attn_norm_g, L0_attn_norm_b, L0_attn_Wq, L0_attn_Wkv, L0_attn_q_scale,
           L0_attn_k_scale, L0_attn_null_kv, L0_attn_Wout, L0_ffn_gate_w, L0_ffn_lb_bias, L0_ffn_w1, L0_ffn_w2,
           L0_ffn_cfc, L0_ffn_cproj):
    import numpy as np
    import concourse.bacc as bacc
    from concourse import mybir as mb
    from concourse.bass_utils import run_bass_kernel_spmd

    values = [x, np.asarray(L0_tok_weight).T, L0_tok_bias, L0_attn_norm_g, L0_attn_norm_b, L0_attn_Wq, L0_attn_Wkv,
              L0_attn_q_scale, L0_attn_k_scale, L0_attn_null_kv, L0_attn_Wout, np.asarray(L0_ffn_gate_w).T, L0_ffn_lb_bias,
              np.asarray(L0_ffn_w1).transpose(0, 2, 1), np.asarray(L0_ffn_w2).transpose(0, 2, 1),
              np.asarray(L0_ffn_cfc).T, np.asarray(L0_ffn_cproj).T]
    nc = bacc.Bacc("TRN2", target_bir_lowering=False, num_devices=1)
    arrays, args = {}, []
    for name, v in zip(_NAMES, values):
        a = np.ascontiguousarray(v)
        arrays[f"in_{name}"] = a
        args.append(nc.dram_tensor(f"in_{name}", a.shape, mb.dt.from_np(a.dtype), kind="ExternalInput").ap())
    shape = (x.shape[0], x.shape[1], L0_tok_weight.shape[0])
    args.append(nc.dram_tensor("out_0", shape, mb.dt.float32, kind="ExternalOutput").ap())
    lm_tower_kernel(nc, *args)
    r = run_bass_kernel_spmd(nc, [arrays], core_ids=[0])
    return r.results[0]["out_0"]
```
